# Optimizing a Trainium2 kernel written in Bass

```python
import numpy as np
import jax
import jax.numpy as jnp

def _softmax(x, axis=-1):
    return jax.nn.softmax(x, axis=axis)

def _gelu(x):
    return jax.nn.gelu(x, approximate=True)

def _silu(x):
    return jax.nn.silu(x)

def _sigmoid(x):
    return jax.nn.sigmoid(x)

def _layernorm(x, axis=-1, eps=1e-05):
    m = jnp.mean(x, axis=axis, keepdims=True)
    v = jnp.var(x, axis=axis, keepdims=True)
    return (x - m) / jnp.sqrt(v + eps)

def _scatter_add(tgt, idx, src, axis=0):
    return tgt.at[idx].add(src)

def _segment_sum(src, seg, n):
    return jax.ops.segment_sum(src, seg, n)
kernel_name = 'mk_adj_preln_d2_adj_r2_6acee7'

def setup_inputs(seed: int=0):
    np.random.seed(seed)
    _w = jnp.asarray

    def _rec_inputs():
        import jax
        import jax.numpy as jnp
        _gk = jax.random.key(seed)
        x = -0.006082 + 1.001 * jax.random.normal(jax.random.fold_in(_gk, 1), (8192, 64), jnp.float32)
        _a = jax.random.bernoulli(jax.random.fold_in(_gk, 2), 0.00195312, (8192, 8192))
        adj = _a.astype(jnp.int32)
        return (x, adj)
    x, adj = _rec_inputs()

    def _L0_gnn_setup():
        import jax, jax.numpy as jnp
        import numpy as np
        ALPHA = 0.2
        NEG_INF = -9000000000000000.0
        key = jax.random.key(seed)
        k1, k2, k3, k4 = jax.random.split(key, 4)
        N, F_IN, F_OUT = (512, 64, 64)
        h = jax.random.normal(k1, (N, F_IN), dtype=jnp.float32)
        adj = jax.random.randint(k2, (N, N), 0, 2, dtype=jnp.int32)
        lim_W = 1.414 * np.sqrt(6.0 / (F_IN + F_OUT))
        W = jax.random.uniform(k3, (F_IN, F_OUT), minval=-lim_W, maxval=lim_W, dtype=jnp.float32)
        lim_a = 1.414 * np.sqrt(6.0 / (2 * F_OUT + 1))
        a = jax.random.uniform(k4, (2 * F_OUT, 1), minval=-lim_a, maxval=lim_a, dtype=jnp.float32)
        return {'h': h, 'adj': adj, 'W': W, 'a': a}
    _L0_gnn_all = _L0_gnn_setup()
    _L0_gnn_in = {k: v for k, v in _L0_gnn_all.items() if k in ('W', 'a')}
    del _L0_gnn_all

    def _L1_gnn_setup():
        import jax, jax.numpy as jnp
        import numpy as np
        N = 8192
        D = 64
        key = jax.random.key(seed)
        k1, k2, k3 = jax.random.split(key, 3)
        x = jax.random.normal(k1, (N, D), dtype=jnp.float32)
        adj_mat = jax.random.randint(k2, (N, N), 0, 2, dtype=jnp.int32)
        U = jax.random.normal(k3, (D, D), dtype=jnp.float32)
        return {'x': x, 'adj_mat': adj_mat, 'U': U}
    _L1_gnn_all = _L1_gnn_setup()
    _L1_gnn_in = {k: v for k, v in _L1_gnn_all.items() if k in ('U',)}
    del _L1_gnn_all
    return {'x': x, 'adj': adj, 'L0_gnn_W': _L0_gnn_in['W'], 'L0_gnn_a': _L0_gnn_in['a'], 'L1_gnn_U': _L1_gnn_in['U']}

def reference(x, adj, L0_gnn_W, L0_gnn_a, L1_gnn_U):
    import jax
    import jax.numpy as jnp

    def _L0_gnn_ref(h, adj, W, a):
        import jax, jax.numpy as jnp
        import numpy as np
        ALPHA = 0.2
        NEG_INF = -9000000000000000.0
        F_OUT = W.shape[1]
        Wh = h @ W
        a1, a2 = (a[:F_OUT, 0], a[F_OUT:, 0])
        e = (Wh @ a1)[:, None] + (Wh @ a2)[None, :]
        e = jax.nn.leaky_relu(e, negative_slope=ALPHA)
        scores = jnp.where(adj > 0, e, jnp.float32(NEG_INF))
        attention = jax.nn.softmax(scores, axis=1)
        h_prime = attention @ Wh
        return jax.nn.elu(h_prime)

    def _L1_gnn_ref(x, adj_mat, U):
        import jax, jax.numpy as jnp
        import numpy as np
        N = 8192
        D = 64
        a = adj_mat.astype(x.dtype)
        deg = a.sum(axis=0)
        agg = jnp.einsum('ji,jd->id', a, x)
        out = jax.nn.relu(agg @ U.T / deg[:, None])
        return out
    h = jnp.maximum(_layernorm(x, axis=-1), 0.0)
    x = x + _L0_gnn_ref(h, adj, L0_gnn_W, L0_gnn_a)
    h = jnp.maximum(_layernorm(x, axis=-1), 0.0)
    x = x + _L1_gnn_ref(h, adj, L1_gnn_U)
    return x

_drawn_inputs = setup_inputs


def setup_inputs(seed=0):
    import zlib

    import numpy as np

    out = dict(_drawn_inputs(seed))
    spreads = {}
    factors = {}
    for name, (base, spread) in spreads.items():
        noise = np.random.default_rng([zlib.crc32(name.encode()), seed]).standard_normal(out[name].shape)
        drawn = base * np.exp(spread * noise) if base else spread * noise
        out[name] = jnp.asarray(drawn.astype(out[name].dtype))
    for name, factor in factors.items():
        out[name] = (out[name] * factor).astype(out[name].dtype)
    return out
```

```python
from contextlib import ExitStack

import concourse.bass as bass
from concourse import mybir

P = 128
N = 8192
D = 64
NB = N // P
B = 4
NS = NB // B
UNIT = 2048
UB = N // UNIT
UT = UNIT // P
NU = NB * UB
US = B * UB
SLOTS = 12
BODY = SLOTS * UB
LAG = US + 8
NL = NU + LAG
DX = D + 1
VW = 2 * DX
QR = 3
GT = 2
HW = D + 1 + D
GW = GT * HW
STAGE = 4
EPS = 1e-5
SLOPE = 0.2
LOW = 2.0 ** 11
VMAX = 2.0 ** 14
HSCALE = 2.0 ** 11
ONE8 = 56.0

F32 = mybir.dt.float32
F16 = mybir.dt.float16
BF16 = mybir.dt.bfloat16
F8 = mybir.dt.float8e4
U8 = mybir.dt.uint8
ALU = mybir.AluOpType
ACT = mybir.ActivationFunctionType
AX = mybir.AxisListType


def build(nc, x, adj, W, a, U, x1_dram, t_dram, out):
    with ExitStack() as ctx:
        signals = {}

        def sb(name, shape, dt):
            return ctx.enter_context(nc.sbuf_tensor(name, shape, dt))

        def sem(name):
            if name not in signals:
                signals[name] = ctx.enter_context(nc.semaphore(name))
            return signals[name]

        ring = sb("adj_ring", [P, SLOTS * N], F8)
        tb = sb("t_rows", [P, N], F32)
        V = sb("V", [P, NB, 2 * VW], F16)
        acc = sb("sums", [P, NB, DX], F32)
        Q = sb("coded", [P, QR, UNIT], BF16)
        M = sb("masks", [P, 2, 2, UNIT], BF16)
        stage = sb("stage", [P, STAGE, GT, HW], F32)
        att = sb("att", [P, B, 2, VW], F32)
        h2 = sb("h2", [P, 3, B, HW], F16)
        xb = sb("xb", [P, B, D], F32)
        p1 = sb("p1", [P, B, D], F32)
        p2 = sb("p2", [P, B, D], F32)
        small = sb("small", [P, 8, B], F32)
        ns = sb("neg_s", [P, NB], F32)
        alpha = sb("alpha", [P, NB], F32)
        beta = sb("beta", [P, NB], F32)
        ident = sb("ident", [P, P], BF16)
        identf = sb("identf", [P, P], F32)
        UTx = sb("UT_blocks", [P, P], F32)
        meanW = sb("mean_Wh", [P, D], F32)
        cst = sb("consts", [P, 16], F32)
        m56, neg_T, neg_T2, g_inv, t_max = (cst[:, i:i + 1] for i in range(5))

        def over(start, parts, *shape):
            size = 4
            for n in shape:
                size *= n
            flat = ring[0:parts, start:start + size].bitcast(F32)
            if len(shape) == 2:
                flat = flat.rearrange("p (a b) -> p a b", a=shape[0])
            if len(shape) == 3:
                flat = flat.rearrange("p (a b c) -> p a b c", a=shape[0], b=shape[1])
            return flat

        xs = over(4 * N, P, NB, D)
        sq = over(6 * N, P, NB, D)
        hT = over(6 * N, P, NB // 2, P)
        Wh = over(8 * N, P, NB, D + 2)
        vt = [over(4 * N, P, 2, UT, DX), over(6 * N, P, 2, UT, DX)]
        at = 8 * N + 4 * NB * (D + 2)
        e1, e2, z, v0, v1, v2, v3, hsum = (over(at + 256 * i, P, NB) for i in range(8))
        at += 8 * 256
        Wx = over(at, P, 2 * (D + 2))
        WT2, UU = over(at + 576, D, P), over(at + 1088, D, P)
        a12, Wsq, tT = over(at + 1600, D, 2), over(at + 1664, D, D), over(at + 1920, D, P)
        ones, hs2 = over(at + 2432, P, P), over(at + 2944, P, P)
        tm, stT = over(at + 3456, P, 1), over(at + 3460, 1, 1)

        x1s = over(4 * N, P, NB, D)
        outs = over(6 * N, P, NB, D)
        fin = over(8 * N, P, 2, 8, D)
        aggT = over(8 * N + 4096, P, 2, 512)
        rdeg, rzero = over(9 * N, P, NB), over(9 * N + 256, P, NB)

        psT = ctx.enter_context(nc.psum_tensor("psT", [P, 4, 512], F32))
        psA = ctx.enter_context(nc.psum_tensor("psA", [P, 2, 512], F32))
        psL = ctx.enter_context(nc.psum_tensor("psL", [P, 2, 512], F32))
        pT = [psT[:, 2 * i:2 * i + 2, :].rearrange("p b n -> p (b n)").bitcast(BF16) for i in range(2)]

        q_ready, t_ready = sem("q_ready"), sem("t_ready")
        m1_ready, m2_ready = sem("m1_ready"), sem("m2_ready")
        l1_done, att_ready = sem("l1_done"), sem("att_ready")
        l2_done, stage_ready = sem("l2_done"), sem("stage_ready")
        added = sem("added")
        landed = [sem(f"adj_landed{i}") for i in range(SLOTS)]

        def after(eng, signal, count):
            if not isinstance(count, int) or count > 0:
                eng.wait_ge(signal, count)

        def place(lap, r):
            lap, r = lap + r // BODY, r % BODY
            return lap, r, lap * BODY + r, lap * SLOTS + r // UB, lap * (BODY // US) + r // US

        def columns(v, lo, hi, width):
            return v[:, lo:hi].unsqueeze(2).broadcast_to([P, hi - lo, width])

        def groups(k, n):
            return [(g, slice(n // k * g, n // k * (g + 1))) for g in range(k)]

        block = ctx.enter_context(nc.Block())

        @block.sync
        def _(sp):
            xg = x.rearrange("(g b p) d -> g p b d", p=P, g=4)
            with nc.allow_non_contiguous_dma(reason="128 numbers"):
                sp.dma_start(a12, a.rearrange("(t f) o -> f (t o)", t=2)).then_inc(sem("w_landed"), 16)
            sp.wait_ge(sem("i_zeros"), 2)
            sp.dma_start(Wx[0:D, 0:D], W).then_inc(sem("w_landed"), 16)
            sp.dma_start(Wx[D:P, D + 2:2 * D + 2], W).then_inc(sem("w_landed"), 16)
            sp.dma_start(xs[:, 0:16, :], xg[0]).then_inc(sem("x_landed0"), 16)
            sp.dma_start(xs[:, 32:48, :], xg[2]).then_inc(sem("x_landed2"), 16)
            sp.dma_start(UU[:, 0:D], U).then_inc(sem("u_landed"), 16)
            sp.dma_start(UU[:, D:P], U).then_inc(sem("u_landed"), 16)
            sp.wait_ge(sem("i_tT"), 1)
            sp.dma_start(t_dram, tT).then_inc(sem("t_stored"), 16)
            sp.wait_ge(sem("t_stored"), 16)
            for c in range(UB):
                row = t_dram.rearrange("b p -> (b p)").unsqueeze(0)[:, UNIT * c:UNIT * c + UNIT]
                sp.dma_start(tb[:, UNIT * c:UNIT * c + UNIT], row.broadcast_to([P, UNIT])).then_inc(sem(f"tb_landed{c}"), 16)
            xv = x.rearrange("(s b p) d -> p s b d", p=P, b=B)
            x1v = x1_dram.rearrange("(s b p) d -> p s b d", p=P, b=B)
            for s in range(NS):
                if s:
                    sp.wait_ge(sem("p_xc"), s)
                    sp.wait_ge(sem("d_sum"), s)
                    sp.wait_ge(sem("x1_stored"), 16 * s)
                sp.dma_start(xb[:], xv[:, s]).then_inc(sem("xb_landed"), 16)
                sp.wait_ge(sem("p_x1"), s + 1)
                sp.dma_start(x1v[:, s], xb[:]).then_inc(sem("x1_stored"), 16)
            sp.wait_ge(sem("x1_stored"), 16 * NS)
            sp.wait_ge(l2_done, 2 * US * (NS - 2))
            sp.dma_start(x1s, x1_dram.rearrange("(b p) d -> p b d", p=P)).then_inc(sem("x1_back"), 16)
            ov = out.rearrange("(f b p) d -> p f b d", p=P, b=8)
            for f in range(8):
                sp.wait_ge(sem("f_out"), f + 1)
                sp.dma_start(ov[:, f], outs[:, 8 * f:8 * f + 8, :]).then_inc(sem("out_stored"), 16)
            sp.wait_ge(sem("out_stored"), 16 * 8)

        @block.gpsimd
        def _(pool):
            def load(n):
                slot = n % SLOTS
                pool.dma_start(ring[:, slot * N:(slot + 1) * N], adj[n * P:(n + 1) * P, :],
                               max_dma_last_dim=8192).then_inc(landed[slot], 16)

            pool.memset(UTx[:], 0.0).then_inc(sem("i_zeros"), 1)
            load(0)
            pool.memset(ident[:], 0.0).then_inc(sem("i_zero"), 1)
            pool.memset(identf[:], 0.0).then_inc(sem("i_zero"), 1)
            pool.wait_ge(sem("i_zero"), 2)
            for m in (ident, identf):
                pool.affine_select(out=m[:], in_=m[:], compare_op=ALU.not_equal, fill=1.0, base=0,
                                   pattern=[[-1, P]], channel_multiplier=1).then_inc(sem("i_ident"), 1)
            for n in range(1, B):
                load(n)
            pool.memset(acc[:], 0.0).then_inc(added, 1)
            pool.memset(h2[:], HSCALE).then_inc(sem("i_h2"), 1)
            for g in (1, 3):
                bl = slice(16 * g, 16 * g + 16)
                pool.wait_ge(sem("i_mean"), g + 1)
                pool.tensor_tensor(xs[:, bl, :], xs[:, bl, :], columns(v1, bl.start, bl.stop, D),
                                   ALU.subtract).then_inc(sem("i_xc_pool"), 1)
            pool.wait_ge(sem("i_rstd"), 1)
            bl = slice(48, 64)
            pool.tensor_tensor(xs[:, bl, :], xs[:, bl, :], columns(v3, bl.start, bl.stop, D),
                               ALU.mult).then_inc(sem("i_h3"), 1)
            pool.wait_ge(sem("i_ev"), 2)
            for c in range(4):
                tiles = slice(UT * c, UT * c + UT)
                if c >= 2:
                    pool.wait_ge(sem("v_lo"), 2 * (c - 1))
                pool.tensor_tensor(vt[c % 2][:, 1, :, 0:D], Wh[:, tiles, 0:D],
                                   columns(v2, tiles.start, tiles.stop, D), ALU.mult).then_inc(sem("v_t2"), 1)
            pool.wait_ge(sem("i_done_dve"), 1)
            pool.wait_ge(sem("i_done_act"), 1)
            for n in range(B, SLOTS):
                load(n)

            def add(j):
                for g in (2 * j, 2 * j + 1):
                    ct = GT * (g % (NB // GT))
                    st = stage[:, g % STAGE]
                    pool.wait_ge(stage_ready, g + 1)
                    pool.wait_ge(added, 1 + 2 * max(0, g - NB // GT + 1))
                    pool.tensor_tensor(acc[:, ct:ct + GT, :], acc[:, ct:ct + GT, :], st[:, :, 0:DX],
                                       ALU.add).then_inc(added, 1)
                    pool.wait_ge(added, 1 + 2 * g + 1)
                    pool.tensor_tensor(acc[:, ct:ct + GT, 0:D], acc[:, ct:ct + GT, 0:D], st[:, :, DX:HW],
                                       ALU.add).then_inc(added, 1)

            flag, den, den_g, mean, rstd, recip, total, var = (small[:, i, :] for i in range(8))

            def over_d(v):
                return v.unsqueeze(2).broadcast_to([P, B, D])

            def post(s, k):
                def need(name):
                    pool.wait_ge(sem(name), s + 1)

                def tt(out_, in0, in1, op, name):
                    pool.tensor_tensor(out_, in0, in1, op).then_inc(sem(name), 1)

                def ts(out_, in_, c0, c1, op0, op1, name):
                    if c1 is None:
                        pool.tensor_scalar(out_, in_, c0, None, op0).then_inc(sem(name), 1)
                    else:
                        pool.tensor_scalar(out_, in_, c0, c1, op0, op1).then_inc(sem(name), 1)

                low, v = att[:, :, 1, 0:DX], att[:, :, 1, DX:VW]
                if k == 0:
                    pool.wait_ge(att_ready, 2 * B * (s + 1))
                    tt(att[:, :, 0, :], att[:, :, 0, :], att[:, :, 1, :], ALU.add, "p_w")
                    need("p_w")
                    ts(low, att[:, :, 0, DX:VW], 1 / LOW, 1.0, ALU.mult, ALU.mult, "p_lo")
                    need("p_lo")
                    tt(v, att[:, :, 0, 0:DX], low, ALU.add, "p_v")
                    need("p_v")
                    ts(flag, v[:, :, D], 0.0, None, ALU.is_equal, None, "p_flag")
                    need("p_flag")
                    tt(den, v[:, :, D], flag, ALU.add, "p_den")
                    need("p_den")
                    ts(den_g, den, g_inv, 1.0, ALU.mult, ALU.mult, "p_den_g")
                if k == 1:
                    tt(p1[:], meanW[:].unsqueeze(1).broadcast_to([P, B, D]), over_d(flag), ALU.mult, "p_nf")
                    need("p_nf")
                    tt(p1[:], p1[:], v[:, :, 0:D], ALU.add, "p_num")
                    need("p_num")
                    need("d_recip")
                    tt(p1[:], p1[:], over_d(recip), ALU.mult, "p_hp")
                    need("p_hp")
                    ts(p2[:], p1[:], 0.0, -3e38, ALU.min, ALU.max, "p_mn")
                if k == 2:
                    need("p_mn")
                    tt(p1[:], p1[:], p2[:], ALU.subtract, "p_mx")
                    need("p_mx")
                    need("a_exp")
                    ts(p2[:], p2[:], -1.0, 1.0, ALU.add, ALU.mult, "p_em1")
                    need("p_em1")
                    tt(p1[:], p1[:], p2[:], ALU.add, "p_elu")
                    need("p_elu")
                    pool.wait_ge(sem("xb_landed"), 16 * (s + 1))
                    tt(xb[:], xb[:], p1[:], ALU.add, "p_x1")
                if k == 3:
                    need("d_mean")
                    tt(p1[:], xb[:], over_d(mean), ALU.subtract, "p_xc")
                    need("p_xc")
                    tt(p2[:], p1[:], p1[:], ALU.mult, "p_sq")
                if k == 5:
                    need("a_relu")
                    need("d_rstd_step_done")
                    hi, lo = h2[:, s % 3, :, 0:D], h2[:, s % 3, :, DX:HW]
                    pool.wait_ge(sem("i_h2"), 1)
                    if s >= 3:
                        pool.wait_ge(l2_done, 2 * US * (s - 2))
                    tt(hi, p1[:], over_d(rstd), ALU.mult, "p_hi")
                    tt(p2[:], p1[:], over_d(rstd), ALU.mult, "p_h")
                    need("p_hi")
                    need("p_h")
                    tt(lo, p2[:], hi, ALU.subtract, "h2_ready")

            for u in range(US, NL + 2):
                j = u - LAG - 2
                if 0 <= j < NU - US:
                    add(j)
                s, k = divmod(u - US - 1, US)
                if 0 <= s < NS:
                    post(s, k)
                if j >= 0 and j % US == US - 1 and B * (j // US) + SLOTS < NB:
                    pool.wait_ge(l2_done, 2 * US * (j // US + 1))
                    for n in range(B * (j // US) + SLOTS, B * (j // US) + SLOTS + B):
                        load(n)

            pool.wait_ge(sem("x1_back"), 16)
            for f in range(8):
                tiles = slice(8 * f, 8 * f + 8)
                pool.wait_ge(sem("f_rdeg"), f + 1)
                pool.tensor_scalar(rzero[:, tiles], rdeg[:, tiles], 0.0, 1.0, ALU.mult,
                                   ALU.mult).then_inc(sem("f_rzero"), 1)
                pool.wait_ge(sem("f_rzero"), f + 1)
                pool.tensor_tensor(x1s[:, tiles, :], x1s[:, tiles, :], columns(rzero, tiles.start, tiles.stop, D),
                                   ALU.add).then_inc(sem("f_x1"), 1)

        @block.vector
        def _(dve):
            def need(name, count=1):
                dve.wait_ge(sem(name), count)

            def rsqrt(y, v, tmp, name, shape_first=0):
                i32 = mybir.dt.int32
                n = shape_first
                dve.tensor_scalar(y.bitcast(i32), v.bitcast(i32), 1, None, ALU.logical_shift_right).then_inc(sem(name), 1)
                need(name, n + 1)
                dve.tensor_scalar(y.bitcast(i32), y.bitcast(i32), -1.0, 1597463007.0, ALU.mult,
                                  ALU.add).then_inc(sem(name), 1)
                for i in range(3):
                    need(name, n + 3 * i + 2)
                    dve.scalar_tensor_tensor(out=tmp, in0=y, scalar=-0.5, in1=y, op0=ALU.mult,
                                             op1=ALU.mult).then_inc(sem(name), 1)
                    need(name, n + 3 * i + 3)
                    dve.tensor_tensor(tmp, tmp, v, ALU.mult).then_inc(sem(name), 1)
                    need(name, n + 3 * i + 4)
                    dve.scalar_tensor_tensor(out=y, in0=tmp, scalar=1.5, in1=y, op0=ALU.add,
                                             op1=ALU.mult).then_inc(sem(name if i < 2 else name + "_done"), 1)

            dve.memset(Wx, 0.0).then_inc(sem("i_zeros"), 1)
            dve.memset(m56, -ONE8).then_inc(sem("i_m56"), 1)
            dve.memset(ones, 1.0).then_inc(sem("i_ones"), 1)
            for g, bl in groups(4, NB):
                need(f"x_landed{g}", 16)
                dve.tensor_reduce(v0[:, bl], xs[:, bl, :], AX.X, ALU.add).then_inc(sem("i_sum"), 1)
                need("i_sum", g + 1)
                dve.tensor_scalar(v1[:, bl], v0[:, bl], 1 / D, None, ALU.mult).then_inc(sem("i_mean"), 1)
                if g % 2 == 0:
                    need("i_mean", g + 1)
                    dve.tensor_tensor(xs[:, bl, :], xs[:, bl, :], columns(v1, bl.start, bl.stop, D),
                                      ALU.subtract).then_inc(sem("i_xc_dve"), 1)
            need("i_ps_WT")
            dve.tensor_copy(WT2[:, 0:D], psA[0:D, 0, 0:D]).then_inc(sem("i_WT"), 1)
            dve.tensor_copy(WT2[:, D:P], psA[0:D, 0, 0:D]).then_inc(sem("i_WT"), 1)
            dve.tensor_tensor(Wsq, Wx[0:D, 0:D], Wx[0:D, 0:D], ALU.mult).then_inc(sem("i_Wsq"), 1)
            for g, bl in groups(4, NB):
                need("i_sq", g + 1)
                dve.tensor_reduce(v2[:, bl], sq[:, bl, :], AX.X, ALU.add).then_inc(sem("i_sumsq"), 1)
            need("i_sumsq", 4)
            dve.tensor_scalar(v2, v2, 1 / D, EPS, ALU.mult, ALU.add).then_inc(sem("i_var"), 1)
            need("i_var")
            rsqrt(v3, v2, v0, "i_rstd_step")
            need("i_rstd_step_done")
            dve.tensor_copy(v1, v3).then_inc(sem("i_rstd"), 1)
            for g, bl in groups(4, NB):
                if g < 3:
                    dve.tensor_tensor(xs[:, bl, :], xs[:, bl, :], columns(v3, bl.start, bl.stop, D),
                                      ALU.mult).then_inc(sem("i_h"), 1)
            need("i_ps_UT")
            dve.tensor_copy(UTx[0:D, 0:D], psL[0:D, 0, 0:D]).then_inc(sem("i_UT"), 1)
            dve.tensor_copy(UTx[D:P, D:P], psL[D:P, 0, 0:D]).then_inc(sem("i_UT"), 1)
            need("i_ps_Wa")
            dve.tensor_copy(Wx[0:D, D:D + 2], psA[0:D, 1, 0:2]).then_inc(sem("i_Wa"), 1)
            dve.tensor_copy(Wx[D:P, 2 * D + 2:2 * D + 4], psA[D:P, 1, 0:2]).then_inc(sem("i_Wa"), 1)
            i32 = mybir.dt.int32
            need("i_ps_norm")
            dve.tensor_reduce(t_max, psL[:, 1, 0:D], AX.X, ALU.max).then_inc(sem("i_g"), 1)
            need("i_g", 1)
            dve.tensor_scalar(t_max, t_max, 1e-30, None, ALU.max).then_inc(sem("i_g"), 1)
            need("i_g", 2)
            dve.tensor_scalar(g_inv.bitcast(i32), t_max.bitcast(i32), 1, None, ALU.logical_shift_right).then_inc(sem("i_g"), 1)
            need("i_g", 3)
            dve.tensor_scalar(g_inv.bitcast(i32), g_inv.bitcast(i32), -1.0, 1597463007.0, ALU.mult,
                              ALU.add).then_inc(sem("i_g"), 1)
            need("i_g", 4)
            dve.tensor_scalar(g_inv, g_inv, 1 / 8.5, None, ALU.mult).then_inc(sem("i_g"), 1)
            for g in range(0, 16, 2):
                need("i_ps_Wh", g + 1)
                dve.tensor_copy(Wh[:, 4 * g:4 * g + 4, :].rearrange("p b n -> p (b n)"),
                                psA[:, 0, 0:4 * (D + 2)]).then_inc(sem("i_Wh_even"), 1)
            need("i_Wh_even", 8)
            need("i_Wh_odd", 8)
            dve.tensor_reduce(tm, Wh[:, :, D + 1], AX.X, ALU.max).then_inc(sem("i_tm"), 1)
            need("i_ps_tm")
            dve.tensor_reduce(stT, psL[0:1, 1, 0:P], AX.X, ALU.max).then_inc(sem("i_stT"), 1)
            need("i_ps_tT")
            dve.tensor_copy(tT, psL[0:D, 0, 0:P]).then_inc(sem("i_tT"), 1)
            dve.tensor_scalar(ns[:], Wh[:, :, D], -1.0, None, ALU.mult).then_inc(sem("i_neg_s"), 1)
            need("i_ps_T")
            dve.tensor_scalar(neg_T, psL[:, 1, 0:1], -1.0, None, ALU.mult).then_inc(sem("i_neg_T"), 1)
            dve.tensor_scalar(neg_T2, psL[:, 1, 0:1], -SLOPE, None, ALU.mult).then_inc(sem("i_neg_T"), 1)
            dve.tensor_copy(t_max, psL[:, 1, 0:1]).then_inc(sem("i_tmax"), 1)
            need("i_tmax")
            dve.tensor_scalar(z, Wh[:, :, D], t_max, 1.0 - SLOPE, ALU.add, ALU.mult).then_inc(sem("i_z"), 1)
            need("i_z")
            dve.tensor_scalar(alpha[:], z, 0.0, None, ALU.min).then_inc(sem("i_z_alpha"), 1)
            dve.tensor_scalar(beta[:], z, -1.0, 0.0, ALU.mult, ALU.min).then_inc(sem("i_z_beta"), 1)

            def coded(lap, r):
                lap, r, u, n, _ = place(lap, r)
                slot, c = r // UB, r % UB
                if c == 0:
                    dve.wait_ge(landed[slot], 16 * (lap + 1))
                if isinstance(u, int) and u < UB:
                    need(f"tb_landed{u}", 16)
                after(dve, t_ready, u - QR + 1)
                dve.scalar_tensor_tensor(
                    out=Q[:, r % QR, :], in0=tb[:, UNIT * c:UNIT * c + UNIT], scalar=ns[:, bass.ds(n, 1)],
                    in1=ring[:, slot * N + UNIT * c:slot * N + UNIT * (c + 1)].bitcast(U8),
                    op0=ALU.is_gt, op1=ALU.add).then_inc(q_ready, 1)

            def mask2(lap, r):
                lap, r, u, _, _ = place(lap, r)
                dve.wait_ge(m1_ready, u + 1)
                dve.tensor_scalar(M[:, r % 2, 1, :], pT[r % 2], ONE8, None,
                                  ALU.is_equal).then_inc(m2_ready, 1)

            def post(lap, r):
                s, k = place(lap, r)[4] - 1, r % US
                recip, total, var, mean, rstd = (small[:, i, :] for i in (5, 6, 7, 3, 4))
                if k == 1:
                    need("p_den_g", s + 1)
                    dve.reciprocal(recip, small[:, 2, :]).then_inc(sem("d_recip"), 1)
                if k == 4:
                    need("p_x1", s + 1)
                    dve.tensor_reduce(total, xb[:], AX.X, ALU.add).then_inc(sem("d_sum"), 1)
                    need("d_sum", s + 1)
                    dve.tensor_scalar(mean, total, 1 / D, None, ALU.mult).then_inc(sem("d_mean"), 1)
                if k == 5:
                    need("p_sq", s + 1)
                    dve.tensor_reduce(total, p2[:], AX.X, ALU.add).then_inc(sem("d_sumsq"), 1)
                    need("d_sumsq", s + 1)
                    dve.tensor_scalar(var, total, 1 / D, EPS, ALU.mult, ALU.add).then_inc(sem("d_var"), 1)
                    need("d_var", s + 1)
                    rsqrt(rstd, var, total, "d_rstd_step", 10 * s)

            need("i_e", 2)
            need("i_g", 5)
            dve.tensor_scalar(v1, e1, g_inv, VMAX * LOW, ALU.mult, ALU.mult).then_inc(sem("i_ev"), 1)
            dve.tensor_scalar(v2, e2, g_inv, VMAX * LOW, ALU.mult, ALU.mult).then_inc(sem("i_ev"), 1)
            need("i_ev", 2)
            need("i_neg_s")
            for c in range(4):
                tiles = slice(UT * c, UT * c + UT)
                buf = vt[c % 2]
                if c >= 2:
                    need("v_lo", 2 * (c - 1))
                for k, e in enumerate((e1, e2)):
                    dve.tensor_scalar(buf[:, k, :, D], e[:, tiles], VMAX * LOW, None, ALU.mult).then_inc(sem("v_te"), 1)
                dve.tensor_tensor(buf[:, 0, :, 0:D], Wh[:, tiles, 0:D], columns(v1, tiles.start, tiles.stop, D),
                                  ALU.mult).then_inc(sem("v_t1"), 1)
                if c == 1:
                    coded(0, 0)
                if c == 3:
                    coded(0, 1)
                for k in range(2):
                    need("v_hi", 2 * c + k + 1)
                    need(("v_t1", "v_t2")[k], c + 1)
                    need("v_te", 2 * c + 2)
                    dve.scalar_tensor_tensor(out=V[:, tiles, VW * k + DX:VW * k + VW],
                                             in0=V[:, tiles, VW * k:VW * k + DX], scalar=-LOW, in1=buf[:, k],
                                             op0=ALU.mult, op1=ALU.add).then_inc(sem("v_lo"), 1)

            def unit(lap, r, ahead=True, post_too=True):
                if ahead:
                    coded(lap, r + 2)
                if post_too:
                    post(lap, r)
                mask2(lap, r)

            need("i_hsum", 8)
            dve.tensor_reduce(v0[:, 0:1], hsum[:, 0:8], AX.X, ALU.add).then_inc(sem("i_htotal"), 1)
            need("i_htotal")
            dve.tensor_scalar(hs2, ones, v0[:, 0:1], None, ALU.mult).then_inc(sem("i_hs2"), 1)
            for r in range(BODY):
                unit(0, r, post_too=r >= US)
                if r == 1:
                    need("i_ps_mean")
                    dve.tensor_scalar(e1, psL[:, 0, 0:D], g_inv, 1 / N, ALU.mult, ALU.mult).then_inc(sem("i_mean_even"), 1)
                    dve.tensor_scalar(e2, psL[:, 0, D + 2:2 * D + 2], g_inv, 1 / N, ALU.mult,
                                      ALU.mult).then_inc(sem("i_mean_odd"), 1)
                    need("i_mean_even")
                    need("i_mean_odd")
                    dve.tensor_tensor(meanW[:], e1, e2, ALU.add).then_inc(sem("i_done_dve"), 1)
            with dve.Fori(1, NU // BODY) as lap:
                for r in range(BODY):
                    unit(lap, r)
            for r in range(NU % BODY):
                unit(NU // BODY, r, ahead=r + 2 < NU % BODY)
            for r in range(US):
                post(NU // BODY, NU % BODY + r)

            for f in range(9):
                for g in range(2 * (NU - US) + 4 * f, 2 * (NU - US) + 4 * f + 4) if f < 8 else ():
                    ct, i = GT * (g % (NB // GT)), g % 2
                    ps = psL[:, i, 0:GW].rearrange("p (t w) -> p t w", w=HW)
                    need("l2_done", g + 1)
                    need("added", 1 + 2 * (g - NB // GT + 1))
                    if g % 4 == 0:
                        after(dve, sem("f_T"), f - 1)
                    dve.tensor_tensor(acc[:, ct:ct + GT, :], acc[:, ct:ct + GT, :], ps[:, :, 0:DX],
                                      ALU.add).then_inc(sem("f_high"), 1)
                    need("f_high", g + 1 - 2 * (NU - US))
                    dve.tensor_tensor(fin[:, f % 2, ct % 8:ct % 8 + GT, :], acc[:, ct:ct + GT, 0:D], ps[:, :, DX:HW],
                                      ALU.add).then_inc(sem("f_added"), 1)
                if f < 8:
                    tiles = slice(8 * f, 8 * f + 8)
                    dve.reciprocal(rdeg[:, tiles], acc[:, tiles, D]).then_inc(sem("f_rdeg"), 1)
                if f:
                    tiles = slice(8 * f - 8, 8 * f)
                    need("f_z", f)
                    need("f_rdeg", f)
                    dve.tensor_tensor(outs[:, tiles, :], psA[:, (f - 1) % 2, :].rearrange("p (t d) -> p t d", t=8),
                                      columns(rdeg, tiles.start, tiles.stop, D), ALU.mult).then_inc(sem("f_mean"), 1)
                    need("f_mean", f)
                    need("f_x1", f)
                    dve.scalar_tensor_tensor(out=outs[:, tiles, :], in0=outs[:, tiles, :], scalar=0.0,
                                             in1=x1s[:, tiles, :], op0=ALU.max, op1=ALU.add).then_inc(sem("f_out"), 1)

        @block.scalar
        def _(act):
            def need(name, count=1):
                act.wait_ge(sem(name), count)

            def wh_out(g):
                need("i_ps_Wh", g + 1)
                act.activation(Wh[:, 4 * g:4 * g + 4, :].rearrange("p b n -> p (b n)"),
                               psA[:, 1, 0:4 * (D + 2)], ACT.Copy).then_inc(sem("i_Wh_odd"), 1)

            xg = x.rearrange("(g b p) d -> g p b d", p=P, g=4)
            for g in (1, 3):
                act.dma_start(xs[:, 16 * g:16 * g + 16, :], xg[g]).then_inc(sem(f"x_landed{g}"), 16)
            for g, bl in groups(4, NB):
                need(("i_xc_dve", "i_xc_pool")[g % 2], g // 2 + 1)
                act.activation(sq[:, bl, :], xs[:, bl, :], ACT.Square).then_inc(sem("i_sq"), 1)
            for g in range(8):
                need("i_ps_hT", g + 1)
                if g == 0:
                    need("i_sumsq", 4)
                act.activation(hT[:, 4 * g:4 * g + 4, :].rearrange("p b n -> p (b n)"), psT[:, g % 4, :],
                               ACT.Relu, accum_out=hsum[:, g:g + 1]).then_inc(sem("i_hsum"), 1)
                if g:
                    wh_out(2 * g - 1)
            wh_out(15)
            need("i_neg_T", 2)
            act.activation(e1, Wh[:, :, D + 1], ACT.Exp, bias=neg_T).then_inc(sem("i_e"), 1)
            act.activation(e2, Wh[:, :, D + 1], ACT.Exp, bias=neg_T2, scale=SLOPE).then_inc(sem("i_e"), 1)
            for c in range(4):
                tiles = slice(UT * c, UT * c + UT)
                for k in range(2):
                    need(("v_t1", "v_t2")[k], c + 1)
                    need("v_te", 2 * c + 2)
                    act.activation(V[:, tiles, VW * k:VW * k + DX], vt[c % 2][:, k], ACT.Copy,
                                   scale=1 / LOW).then_inc(sem("v_hi"), 1)
            need("i_z_beta")
            act.activation(alpha[:], alpha[:], ACT.Exp).then_inc(sem("i_alpha"), 1)
            act.activation(beta[:], beta[:], ACT.Exp).then_inc(sem("i_done_act"), 1)
            need("i_m56")
            need("i_alpha")
            need("i_done_act")

            def mask1(lap, r):
                _, r, u, _, _ = place(lap, r)
                after(act, l1_done, u - 1)
                act.wait_ge(t_ready, u + 1)
                act.activation(M[:, r % 2, 0, :], pT[r % 2], ACT.Relu, bias=m56).then_inc(m1_ready, 1)

            def scaled(lap, r):
                _, r, u, n, s = place(lap, r - UB)
                act.wait_ge(l1_done, u + UB)
                if (r // UB) % B == 0:
                    after(act, sem("p_num"), s)
                for k, factor in enumerate((alpha, beta)):
                    act.activation(att[:, (r // UB) % B, k, :], psA[:, (r // UB) % 2, VW * k:VW * k + VW],
                                   ACT.Copy, scale=factor[:, bass.ds(n, 1)]).then_inc(att_ready, 1)

            def staged(lap, r):
                _, r, u, _, _ = place(lap, r - 1 - LAG)
                for i in range(2):
                    act.wait_ge(l2_done, 2 * u + i + 1)
                    after(act, added, 1 + 2 * (2 * u + i - STAGE + 1))
                    act.activation(stage[:, (2 * r + i) % STAGE].rearrange("p t w -> p (t w)"),
                                   psL[:, i, 0:GW], ACT.Copy).then_inc(stage_ready, 1)

            def post(lap, r):
                s, k = place(lap, r)[4] - 1, r % US
                if k == 2:
                    need("p_mx", s + 1)
                    act.activation(p2[:], p2[:], ACT.Exp).then_inc(sem("a_exp"), 1)
                if k == 5:
                    need("p_sq", s + 1)
                    act.activation(p1[:], p1[:], ACT.Relu, scale=HSCALE).then_inc(sem("a_relu"), 1)

            def unit(lap, r, first=False):
                mask1(lap, r)
                if r % UB == 0 and not (first and r == 0):
                    scaled(lap, r)
                if not first or r > LAG:
                    staged(lap, r)
                if not first or r >= US:
                    post(lap, r)

            for r in range(BODY):
                unit(0, r, first=True)
            with act.Fori(1, NU // BODY) as lap:
                for r in range(BODY):
                    unit(lap, r)
            for r in range(NU % BODY):
                unit(NU // BODY, r)
            for r in range(NU % BODY, NU % BODY + LAG + 1):
                if r == NU % BODY:
                    scaled(NU // BODY, r)
                if r - 1 - LAG < NU % BODY - US:
                    staged(NU // BODY, r)
                if r < NU % BODY + US:
                    post(NU // BODY, r)

            for f in range(8):
                need("f_T", f + 1)
                after(act, sem("f_z"), f - 1)
                act.activation(aggT[:, f % 2, :], psT[:, f % 2, :], ACT.Copy).then_inc(sem("f_aggT"), 1)

        @block.tensor
        def _(pe):
            def need(name, count=1):
                pe.wait_ge(sem(name), count)

            need("i_ident", 2)
            need("w_landed", 48)
            pe.transpose(psA[0:D, 0, 0:D], Wx[0:D, 0:D], identf[0:D, 0:D]).then_inc(sem("i_ps_WT"), 1)
            need("i_WT", 2)
            pe.matmul(psA[:, 1, 0:2], WT2, a12, start=True, stop=True).then_inc(sem("i_ps_Wa"), 1)
            need("i_Wsq")
            need("i_ones")
            pe.matmul(psL[:, 1, 0:D], ones[0:D, :], Wsq, start=True, stop=True).then_inc(sem("i_ps_norm"), 1)
            need("u_landed", 32)
            pe.transpose(psL[:, 0, 0:D], UU, identf[0:D, 0:D]).then_inc(sem("i_ps_UT"), 1)

            def h_transposed(g):
                if g % 2 == 0:
                    need(*(("i_h", g // 2 + 1) if g < 6 else ("i_h3", 1)))
                after(pe, sem("i_hsum"), g - 3)
                for i in range(4):
                    last = pe.transpose(psT[:, g % 4, P * i:P * i + P],
                                        xs[:, 8 * g + 2 * i:8 * g + 2 * i + 2, :].rearrange("p b d -> p (b d)"),
                                        identf[:])
                last.then_inc(sem("i_ps_hT"), 1)

            h_transposed(0)
            for g in range(16):
                if g % 2 == 0:
                    if g < 14:
                        h_transposed(g // 2 + 1)
                    need("i_hsum", g // 2 + 1)
                if g == 0:
                    need("i_Wa", 2)
                if g >= 2:
                    need("i_Wh_odd" if g % 2 else "i_Wh_even", (g - 2) // 2 + 1)
                for i in range(2):
                    last = pe.matmul(psA[:, g % 2, i * 2 * (D + 2):(i + 1) * 2 * (D + 2)], hT[:, 2 * g + i, :], Wx,
                                     start=True, stop=True, skip_group_check=True)
                last.then_inc(sem("i_ps_Wh"), 1)
            need("i_tm")
            need("i_g", 1)
            pe.transpose(psL[0:1, 1, 0:P], tm, identf[:]).then_inc(sem("i_ps_tm"), 1)
            need("i_UT", 2)
            pe.transpose(psL[0:D, 0, 0:P], Wh[:, :, D + 1], identf[:]).then_inc(sem("i_ps_tT"), 1)
            need("i_stT")
            pe.matmul(psL[:, 1, 0:1], ones[0:1, :], stT, start=True, stop=True).then_inc(sem("i_ps_T"), 1)

            def transposes(lap, r):
                _, r, u, _, _ = place(lap, r)
                pe.wait_ge(q_ready, u + 1)
                after(pe, m2_ready, u - 1)
                for i in range(UT):
                    last = pe.transpose(pT[r % 2][:, P * i:P * i + P], Q[:, r % QR, P * i:P * i + P], ident[:])
                last.then_inc(t_ready, 1)

            def attend(lap, r, first):
                _, r, u, n, _ = place(lap, r)
                c = r % UB
                if c == 0:
                    after(pe, att_ready, 2 * (n - 1))
                if first and r < UB:
                    need("v_lo", 2 * (r + 1))
                pe.wait_ge(m2_ready, u + 1)
                for i in range(UT):
                    for k in range(2):
                        last = pe.matmul(psA[:, (r // UB) % 2, VW * k:VW * k + VW],
                                         M[:, r % 2, k, P * i:P * i + P],
                                         V[:, UT * c + i, VW * k:VW * k + VW],
                                         start=(c == 0 and i == 0 and k == 0), stop=(c == UB - 1 and i == UT - 1),
                                         skip_group_check=True)
                last.then_inc(l1_done, 1)

            def sums_wait(lap, r):
                _, r, u, _, s = place(lap, r)
                if r % US == 0:
                    need("h2_ready", s + 1)
                    need("i_done_dve")
                last = NU - US if isinstance(u, int) else NU
                after(pe, stage_ready, min(2 * u, 2 * last) if isinstance(u, int) else 2 * u)
                if isinstance(u, int):
                    after(pe, sem("f_added"), 2 * (u - last))

            def sums(lap, r):
                _, r, u, _, _ = place(lap, r)
                s0 = (r // US) * B
                for i in range(2):
                    for t in range(GT):
                        ct = 2 * GT * (r % US) + GT * i + t
                        for b in range(B):
                            slot = s0 + b
                            last = pe.matmul(psL[:, i, HW * t:HW * t + HW],
                                             ring[:, slot * N + ct * P:slot * N + ct * P + P],
                                             h2[:, (r // US) % 3, b, :],
                                             start=(t == 0 and b == 0), stop=(b == B - 1), skip_group_check=True)
                    last.then_inc(l2_done, 1)

            def unit(lap, r, first=False, ahead=True):
                if ahead:
                    transposes(lap, r + 1)
                two = not first or r >= LAG
                if two:
                    sums_wait(lap, r - LAG)
                attend(lap, r, first)
                if two:
                    sums(lap, r - LAG)

            transposes(0, 0)
            for r in range(BODY):
                unit(0, r, first=True)
                if r == 0:
                    need("i_hs2")
                    need("i_tT")
                    pe.matmul(psL[:, 0, 0:2 * (D + 2)], hs2, Wx, start=True, stop=True).then_inc(sem("i_ps_mean"), 1)
            with pe.Fori(1, NU // BODY) as lap:
                for r in range(BODY):
                    unit(lap, r)
            for r in range(NU % BODY):
                unit(NU // BODY, r, ahead=r + 1 < NU % BODY)
            for r in range(NU % BODY, NU % BODY + LAG - US):
                sums_wait(NU // BODY, r - LAG)
                sums(NU // BODY, r - LAG)

            for f in range(9):
                if f < 8:
                    for r in (NU % BODY - US + 2 * f, NU % BODY - US + 2 * f + 1):
                        sums_wait(NU // BODY, r)
                        sums(NU // BODY, r)
                if f:
                    e = f - 1
                    need("f_added", 4 * f)
                    after(pe, sem("f_aggT"), e - 1)
                    for i in range(4):
                        last = pe.transpose(psT[:, e % 2, P * i:P * i + P],
                                            fin[:, e % 2, 2 * i:2 * i + 2, :].rearrange("p t d -> p (t d)"), identf[:])
                    last.then_inc(sem("f_T"), 1)
                    need("f_aggT", f)
                    after(pe, sem("f_mean"), e - 1)
                    if e == 0:
                        need("att_ready", 2 * NB)
                    for i in range(4):
                        last = pe.matmul(psA[:, e % 2, P * i:P * i + P], aggT[:, e % 2, P * i:P * i + P], UTx[:],
                                         start=True, stop=True, skip_group_check=True)
                    last.then_inc(sem("f_z"), 1)



INPUTS = ["x", "adj", "L0_gnn_W", "L0_gnn_a", "L1_gnn_U"]


def kernel(**inputs):
    import numpy as np
    import concourse.bacc as bacc
    from concourse.bass_utils import run_bass_kernel_spmd

    nc = bacc.Bacc("TRN2", target_bir_lowering=False, num_devices=1, dynamic_dma_scratch_size=2048)
    arrays, args = {}, []
    for name in INPUTS:
        arrays[name] = np.ascontiguousarray(inputs[name])
        args.append(nc.dram_tensor(name, arrays[name].shape, mybir.dt.from_np(arrays[name].dtype),
                                   kind="ExternalInput").ap())
    x1_dram = nc.dram_tensor("x1_dram", (N, D), F32, kind="Internal").ap()
    t_dram = nc.dram_tensor("t_dram", (NB, P), F32, kind="Internal").ap()
    out = nc.dram_tensor("out", (N, D), F32, kind="ExternalOutput").ap()
    build(nc, *args, x1_dram, t_dram, out)
    return run_bass_kernel_spmd(nc, [arrays], core_ids=[0]).results[0]["out"]
```

```python
from contextlib import ExitStack

import concourse.bass as bass
from concourse import mybir

P = 128
N = 8192
D = 64
NB = N // P
B = 4
NS = NB // B
UNIT = 2048
UB = N // UNIT
UT = UNIT // P
NU = NB * UB
US = B * UB
SLOTS = 12
BODY = SLOTS * UB
LAG = US + 8
DIRECT = US + 2
ND = NU - DIRECT
NL = NU + LAG
DX = D + 1
VW = 2 * DX
QR = 3
GT = 2
HW = D + 1 + D
GW = GT * HW
STAGE = 4
EPS = 1e-5
SLOPE = 0.2
LOW = 2.0 ** 11
VMAX = 2.0 ** 15
HSCALE = 2.0 ** 11
ONE8 = 56.0
RSQRT_BITS = 1597463007.0

F32 = mybir.dt.float32
F16 = mybir.dt.float16
BF16 = mybir.dt.bfloat16
F8 = mybir.dt.float8e4
U8 = mybir.dt.uint8
I32 = mybir.dt.int32
ALU = mybir.AluOpType
ACT = mybir.ActivationFunctionType
AX = mybir.AxisListType


def build(nc, x, adj, W, a, U, x1_dram, t_dram, out):
    with ExitStack() as ctx:
        signals = {}

        def sb(name, shape, dt):
            return ctx.enter_context(nc.sbuf_tensor(name, shape, dt))

        def sem(name):
            if name not in signals:
                signals[name] = ctx.enter_context(nc.semaphore(name))
            return signals[name]

        ring = sb("adj_ring", [P, SLOTS * N], F8)
        tb = sb("t_rows", [P, N], F32)
        V = sb("V", [P, NB, 2 * VW], F16)
        acc = sb("sums", [P, NB, DX], F32)
        Q = sb("coded", [P, QR, UNIT], BF16)
        M = sb("masks", [P, 2, 2, UNIT], BF16)
        stage = sb("stage", [P, STAGE, GT, HW], F32)
        att = sb("att", [P, B, 2, VW], F32)
        h2 = sb("h2", [P, 3, B, HW], F16)
        xb = sb("xb", [P, B, D], F32)
        p1 = sb("p1", [P, B, D], F32)
        p2 = sb("p2", [P, B, D], F32)
        p3 = att[:, :, 0, 0:D]
        small = sb("small", [P, 8, B], F32)
        ns = sb("neg_s", [P, NB], F32)
        alpha = sb("alpha", [P, NB], F32)
        beta = sb("beta", [P, NB], F32)
        ident = sb("ident", [P, P], BF16)
        identf = sb("identf", [P, P], F32)
        UTx = sb("UT_blocks", [P, P], F32)
        meanW = sb("mean_Wh", [P, D], F32)
        cst = sb("consts", [P, 16], F32)
        m56, neg_T, neg_T2, g_inv, t_max, norm = (cst[:, i:i + 1] for i in range(6))

        def over(start, parts, *shape):
            size = 4
            for n in shape:
                size *= n
            flat = ring[0:parts, start:start + size].bitcast(F32)
            if len(shape) == 2:
                flat = flat.rearrange("p (a b) -> p a b", a=shape[0])
            if len(shape) == 3:
                flat = flat.rearrange("p (a b c) -> p a b c", a=shape[0], b=shape[1])
            return flat

        xs = over(4 * N, P, NB, D)
        hT = over(6 * N, P, NB // 2, P)
        sq = acc[:, :, 0:D]
        Wh = over(8 * N, P, NB, D + 2)
        vt = [over(4 * N, P, 2, UT, DX), over(6 * N, P, 2, UT, DX)]
        at = 8 * N + 4 * NB * (D + 2)
        e1, e2, z, total0, mean0, var0, rstd0, s0, t0, ev1, ev2, rs1, rs2 = (over(at + 256 * i, P, NB) for i in range(13))
        at += 13 * 256
        Wx = over(at, P, 2 * (D + 2))
        WT2, UU = over(at + 576, D, P), over(at + 1088, D, P)
        a12, Wsq, tT = over(at + 1600, D, 2), over(at + 1664, D, D), over(at + 1920, D, P)
        ones, mean_col = over(at + 2432, P, P), over(at + 2944, D, P)
        tm, stT = over(at + 3456, P, 1), over(at + 3460, 1, 1)

        x1s = over(4 * N, P, NB, D)
        outs = over(6 * N, P, NB, D)
        fin = over(8 * N, P, 2, 8, D)
        aggT = over(8 * N + 4096, P, 2, 512)
        rdeg, rzero = over(9 * N, P, NB), over(9 * N + 256, P, NB)

        psT = ctx.enter_context(nc.psum_tensor("psT", [P, 4, 512], F32))
        psA = ctx.enter_context(nc.psum_tensor("psA", [P, 2, 512], F32))
        psL = ctx.enter_context(nc.psum_tensor("psL", [P, 2, 512], F32))
        pT = [psT[:, 2 * i:2 * i + 2, :].rearrange("p b n -> p (b n)").bitcast(BF16) for i in range(2)]

        q_ready, t_ready = sem("q_ready"), sem("t_ready")
        m1_ready, m2_ready = sem("m1_ready"), sem("m2_ready")
        l1_done, att_ready = sem("l1_done"), sem("att_ready")
        l2_done, stage_ready = sem("l2_done"), sem("stage_ready")
        added = sem("added")
        landed = [sem(f"adj_landed{i}") for i in range(SLOTS)]

        def after(eng, signal, count):
            if not isinstance(count, int) or count > 0:
                eng.wait_ge(signal, count)

        def place(lap, r):
            lap, r = lap + r // BODY, r % BODY
            return lap, r, lap * BODY + r, lap * SLOTS + r // UB, lap * (BODY // US) + r // US

        def columns(v, lo, hi, width):
            return v[:, lo:hi].unsqueeze(2).broadcast_to([P, hi - lo, width])

        def groups(k, n):
            return [(g, slice(n // k * g, n // k * (g + 1))) for g in range(k)]

        block = ctx.enter_context(nc.Block())

        @block.sync
        def _(sp):
            xg = x.rearrange("(g b p) d -> g p b d", p=P, g=4)
            sp.dma_start(xs[:, 0:16, :], xg[0]).then_inc(sem("x_landed0"), 16)
            sp.wait_ge(sem("i_zeros"), 2)
            sp.dma_start(Wx[0:D, 0:D], W).then_inc(sem("w_landed"), 16)
            sp.dma_start(Wx[D:P, D + 2:2 * D + 2], W).then_inc(sem("w_landed"), 16)
            sp.dma_start(xs[:, 32:48, :], xg[2]).then_inc(sem("x_landed2"), 16)
            sp.dma_start(UU[:, 0:D], U).then_inc(sem("u_landed"), 16)
            sp.dma_start(UU[:, D:P], U).then_inc(sem("u_landed"), 16)
            sp.wait_ge(sem("i_tT"), 1)
            sp.dma_start(t_dram, tT).then_inc(sem("t_stored"), 16)
            sp.wait_ge(sem("t_stored"), 16)
            for c in range(UB):
                row = t_dram.rearrange("b p -> (b p)").unsqueeze(0)[:, UNIT * c:UNIT * c + UNIT]
                sp.dma_start(tb[:, UNIT * c:UNIT * c + UNIT], row.broadcast_to([P, UNIT])).then_inc(sem(f"tb_landed{c}"), 16)
            xv = x.rearrange("(s b p) d -> p s b d", p=P, b=B)
            x1v = x1_dram.rearrange("(s b p) d -> p s b d", p=P, b=B)
            for s in range(NS):
                if s:
                    sp.wait_ge(sem("p_xc"), s)
                    sp.wait_ge(sem("d_sum"), s)
                    sp.wait_ge(sem("x1_stored"), 16 * s)
                sp.dma_start(xb[:], xv[:, s]).then_inc(sem("xb_landed"), 16)
                if s < NS - 1:
                    sp.wait_ge(sem("p_x1"), s + 1)
                else:
                    sp.wait_ge(sem("l_x1"), 1)
                sp.dma_start(x1v[:, s], xb[:]).then_inc(sem("x1_stored"), 16)
            sp.wait_ge(sem("x1_stored"), 16 * NS)
            sp.wait_ge(l2_done, 2 * US * (NS - 2))
            sp.dma_start(x1s, x1_dram.rearrange("(b p) d -> p b d", p=P)).then_inc(sem("x1_back"), 16)
            ov = out.rearrange("(f b p) d -> p f b d", p=P, b=8)
            for f in range(8):
                sp.wait_ge(sem("f_out"), f + 1)
                sp.dma_start(ov[:, f], outs[:, 8 * f:8 * f + 8, :]).then_inc(sem("out_stored"), 16)
            sp.wait_ge(sem("out_stored"), 16 * 8)

        @block.gpsimd
        def _(pool):
            def load(n):
                slot = n % SLOTS
                pool.dma_start(ring[:, slot * N:(slot + 1) * N], adj[n * P:(n + 1) * P, :],
                               max_dma_last_dim=8192).then_inc(landed[slot], 16)

            pool.memset(UTx[:], 0.0).then_inc(sem("i_zeros"), 1)
            pool.memset(ident[:], 0.0).then_inc(sem("i_zero"), 1)
            pool.memset(identf[:], 0.0).then_inc(sem("i_zero"), 1)
            pool.wait_ge(sem("i_zero"), 2)
            for m in (identf, ident):
                pool.affine_select(out=m[:], in_=m[:], compare_op=ALU.not_equal, fill=1.0, base=0,
                                   pattern=[[-1, P]], channel_multiplier=1).then_inc(sem("i_ident"), 1)

            def centred(g):
                bl = slice(16 * g, 16 * g + 16)
                pool.wait_ge(sem("i_mean"), g + 1)
                pool.tensor_tensor(xs[:, bl, :], xs[:, bl, :], columns(mean0, bl.start, bl.stop, D),
                                   ALU.subtract).then_inc(sem("i_xc_pool"), 1)

            pool.memset(h2[:], HSCALE).then_inc(sem("i_h2"), 1)
            centred(1)
            pool.wait_ge(sem("x_landed2"), 16)
            pool.wait_ge(sem("x_landed3"), 16)
            load(0)
            centred(3)
            for n in range(1, B):
                load(n)

            def v_product(c):
                tiles = slice(UT * c, UT * c + UT)
                if c >= 2:
                    pool.wait_ge(sem("v_lo2"), c - 1)
                pool.tensor_tensor(vt[c % 2][:, 1, :, 0:D], Wh[:, tiles, 0:D],
                                   columns(ev2, tiles.start, tiles.stop, D), ALU.mult).then_inc(sem("v_t2"), 1)

            def v_rest(c):
                tiles = slice(UT * c, UT * c + UT)
                pool.wait_ge(sem("v_t2"), c + 1)
                pool.wait_ge(sem("v_te2"), c + 1)
                pool.wait_ge(sem("v_hi2"), c + 1)
                pool.tensor_tensor(vt[c % 2][:, 1], vt[c % 2][:, 1], V[:, tiles, VW:VW + DX],
                                   ALU.subtract).then_inc(sem("v_rest2"), 1)

            pool.wait_ge(sem("i_ev"), 1)
            for c in (0, 2):
                v_product(c)
                v_product(c + 1)
                v_rest(c)
                v_rest(c + 1)
            pool.wait_ge(sem("v_lo1"), 4)
            pool.wait_ge(sem("v_lo2"), 4)
            for n in range(B, 2 * B):
                load(n)
            pool.memset(acc[:], 0.0).then_inc(added, 1)
            pool.wait_ge(sem("i_mean_Wh"), 1)
            for n in range(2 * B, SLOTS):
                load(n)

            def add(j):
                for g in (2 * j, 2 * j + 1):
                    ct = GT * (g % (NB // GT))
                    st = stage[:, g % STAGE]
                    pool.wait_ge(stage_ready, g + 1)
                    pool.wait_ge(added, 1 + 2 * max(0, g - NB // GT + 1))
                    pool.tensor_tensor(acc[:, ct:ct + GT, :], acc[:, ct:ct + GT, :], st[:, :, 0:DX],
                                       ALU.add).then_inc(added, 1)
                    pool.wait_ge(added, 1 + 2 * g + 1)
                    pool.tensor_tensor(acc[:, ct:ct + GT, 0:D], acc[:, ct:ct + GT, 0:D], st[:, :, DX:HW],
                                       ALU.add).then_inc(added, 1)

            flag, den, den_g, mean, rstd, recip, total, var = (small[:, i, :] for i in range(8))

            def over_d(v):
                return v.unsqueeze(2).broadcast_to([P, B, D])

            def post(s, k):
                def need(name):
                    pool.wait_ge(sem(name), s + 1)

                def tt(out_, in0, in1, op, name):
                    pool.tensor_tensor(out_, in0, in1, op).then_inc(sem(name), 1)

                def ts(out_, in_, c0, c1, op0, op1, name):
                    if c1 is None:
                        pool.tensor_scalar(out_, in_, c0, None, op0).then_inc(sem(name), 1)
                    else:
                        pool.tensor_scalar(out_, in_, c0, c1, op0, op1).then_inc(sem(name), 1)

                low, v = att[:, :, 1, 0:DX], att[:, :, 1, DX:VW]
                if k == 0:
                    pool.wait_ge(att_ready, 2 * B * (s + 1))
                    tt(att[:, :, 0, :], att[:, :, 0, :], att[:, :, 1, :], ALU.add, "p_w")
                    need("p_w")
                    ts(low, att[:, :, 0, DX:VW], 1 / LOW, 1.0, ALU.mult, ALU.mult, "p_lo")
                    need("p_lo")
                    tt(v, att[:, :, 0, 0:DX], low, ALU.add, "p_v")
                    need("p_v")
                    ts(flag, v[:, :, D], 0.0, None, ALU.is_equal, None, "p_flag")
                    need("p_flag")
                    tt(den, v[:, :, D], flag, ALU.add, "p_den")
                    need("p_den")
                    ts(den_g, den, g_inv, 1.0, ALU.mult, ALU.mult, "p_den_g")
                    tt(p1[:], meanW[:].unsqueeze(1).broadcast_to([P, B, D]), over_d(flag), ALU.mult, "p_nf")
                    need("p_nf")
                    tt(p1[:], p1[:], v[:, :, 0:D], ALU.add, "p_num")
                if k == 1:
                    need("p_num")
                    need("d_recip")
                    tt(p1[:], p1[:], over_d(recip), ALU.mult, "p_hp")
                if k == 2:
                    need("p_hp")
                    need("a_neg")
                    tt(p1[:], p1[:], p2[:], ALU.add, "p_mx")
                    need("p_mx")
                    pool.wait_ge(sem("xb_landed"), 16 * (s + 1))
                    tt(p1[:], xb[:], p1[:], ALU.add, "p_x_mx")
                    need("a_exp")
                    ts(p3, p3, -1.0, 1.0, ALU.add, ALU.mult, "p_em1")
                    need("p_em1")
                    need("p_x_mx")
                    tt(xb[:], p1[:], p3, ALU.add, "p_x1")
                if k == 4:
                    need("d_mean")
                    tt(p1[:], xb[:], over_d(mean), ALU.subtract, "p_xc")
                    need("p_xc")
                    tt(p2[:], p1[:], p1[:], ALU.mult, "p_sq")
                if k == 6:
                    need("d_guess")
                    for n in range(12 * s, 12 * s + 12, 4):
                        if n:
                            pool.wait_ge(sem("p_newton"), n)
                        tt(total, rstd, rstd, ALU.mult, "p_newton")
                        pool.wait_ge(sem("p_newton"), n + 1)
                        tt(total, total, var, ALU.mult, "p_newton")
                        pool.wait_ge(sem("p_newton"), n + 2)
                        ts(total, total, -0.5, 1.5, ALU.mult, ALU.add, "p_newton")
                        pool.wait_ge(sem("p_newton"), n + 3)
                        tt(rstd, rstd, total, ALU.mult, "p_newton")
                if k == 6:
                    need("a_relu")
                    pool.wait_ge(sem("p_newton"), 12 * (s + 1))
                    hi, lo = h2[:, s % 3, :, 0:D], h2[:, s % 3, :, DX:HW]
                    pool.wait_ge(sem("i_h2"), 1)
                    if s >= 3:
                        pool.wait_ge(l2_done, 2 * US * (s - 2))
                    tt(hi, p1[:], over_d(rstd), ALU.mult, "p_hi")
                    tt(p2[:], p1[:], over_d(rstd), ALU.mult, "p_h")
                    need("p_hi")
                    need("p_h")
                    tt(lo, p2[:], hi, ALU.subtract, "h2_ready")

            for u in range(US, NL + 2):
                j = u - LAG - 2
                s, k = divmod(u - US - 1, US)
                if 0 <= s < NS - 1 and k < 2:
                    post(s, k)
                if 0 <= j < ND:
                    add(j)
                if 0 <= s < NS - 1 and k >= 2:
                    post(s, k)
                if j >= 0 and j % US == US - 1 and B * (j // US) + SLOTS < NB:
                    pool.wait_ge(l2_done, 2 * US * (j // US + 1))
                    for n in range(B * (j // US) + SLOTS, B * (j // US) + SLOTS + B):
                        load(n)

            pool.wait_ge(sem("x1_back"), 16)
            for f in range(8):
                tiles = slice(8 * f, 8 * f + 8)
                pool.wait_ge(sem("f_rdeg"), f + 1)
                pool.tensor_scalar(rzero[:, tiles], rdeg[:, tiles], 0.0, 1.0, ALU.mult,
                                   ALU.mult).then_inc(sem("f_rzero"), 1)
                pool.wait_ge(sem("f_rzero"), f + 1)
                pool.tensor_tensor(x1s[:, tiles, :], x1s[:, tiles, :], columns(rzero, tiles.start, tiles.stop, D),
                                   ALU.add).then_inc(sem("f_x1"), 1)

        @block.vector
        def _(dve):
            def need(name, count=1):
                dve.wait_ge(sem(name), count)

            def guess(y, v, half, done, count=0):
                dve.tensor_scalar(y.bitcast(I32), v.bitcast(I32), 1, None,
                                  ALU.logical_shift_right).then_inc(sem(half), 1)
                need(half, count + 1)
                dve.tensor_scalar(y.bitcast(I32), y.bitcast(I32), -1.0, RSQRT_BITS, ALU.mult,
                                  ALU.add).then_inc(sem(done), 1)

            def rsqrt(y, v, tmp, name):
                guess(y, v, name + "_half", name)
                for i in range(3):
                    need(name, 3 * i + 1)
                    dve.scalar_tensor_tensor(out=tmp, in0=y, scalar=-0.5, in1=y, op0=ALU.mult,
                                             op1=ALU.mult).then_inc(sem(name), 1)
                    need(name, 3 * i + 2)
                    dve.tensor_tensor(tmp, tmp, v, ALU.mult).then_inc(sem(name), 1)
                    need(name, 3 * i + 3)
                    dve.scalar_tensor_tensor(out=y, in0=tmp, scalar=1.5, in1=y, op0=ALU.add,
                                             op1=ALU.mult).then_inc(sem(name), 1)

            dve.memset(Wx, 0.0).then_inc(sem("i_zeros"), 1)
            dve.memset(m56, -ONE8).then_inc(sem("i_m56"), 1)
            dve.memset(ones, 1.0).then_inc(sem("i_ones"), 1)

            def Wh_out(g):
                need("i_ps_Wh", g + 1)
                dve.tensor_copy(Wh[:, 4 * g:4 * g + 4, :].rearrange("p b n -> p (b n)"),
                                psA[:, 0, 0:4 * (D + 2)]).then_inc(sem("i_Wh_even"), 1)

            for g, bl in groups(4, NB):
                need(f"x_landed{g}", 16)
                dve.tensor_reduce(total0[:, bl], xs[:, bl, :], AX.X, ALU.add).then_inc(sem("i_sum"), 1)
                need("i_sum", g + 1)
                dve.tensor_scalar(mean0[:, bl], total0[:, bl], 1 / D, None, ALU.mult).then_inc(sem("i_mean"), 1)
                if g % 2 == 0:
                    need("i_mean", g + 1)
                    dve.tensor_tensor(xs[:, bl, :], xs[:, bl, :], columns(mean0, bl.start, bl.stop, D),
                                      ALU.subtract).then_inc(sem("i_xc_dve"), 1)
                if g == 0:
                    need("i_ps_WT")
                    dve.tensor_copy(WT2[:, 0:D], psA[0:D, 0, 0:D]).then_inc(sem("i_WT"), 1)
                    dve.tensor_copy(WT2[:, D:P], psA[0:D, 0, 0:D]).then_inc(sem("i_WT"), 1)
                    dve.tensor_tensor(Wsq, Wx[0:D, 0:D], Wx[0:D, 0:D], ALU.mult).then_inc(sem("i_Wsq"), 1)
                if g == 1:
                    need("i_ps_Wa")
                    dve.tensor_copy(Wx[0:D, D:D + 2], psA[0:D, 1, 0:2]).then_inc(sem("i_Wa"), 1)
                    dve.tensor_copy(Wx[D:P, 2 * D + 2:2 * D + 4], psA[D:P, 1, 0:2]).then_inc(sem("i_Wa"), 1)
                    need("i_ps_norm")
                    dve.tensor_reduce(norm, psL[:, 1, 0:D], AX.X, ALU.max).then_inc(sem("i_g"), 1)
                    need("i_g", 1)
                    dve.tensor_scalar(norm, norm, 1e-30, None, ALU.max).then_inc(sem("i_g"), 1)
                    need("i_g", 2)
                    dve.tensor_scalar(g_inv.bitcast(I32), norm.bitcast(I32), 1, None, ALU.logical_shift_right).then_inc(sem("i_g"), 1)
                    need("i_g", 3)
                    dve.tensor_scalar(g_inv.bitcast(I32), g_inv.bitcast(I32), -1.0, RSQRT_BITS, ALU.mult,
                                      ALU.add).then_inc(sem("i_g"), 1)
                    need("i_g", 4)
                    dve.tensor_scalar(g_inv, g_inv, 1 / 8.5, None, ALU.mult).then_inc(sem("i_g"), 1)
                    Wh_out(0)
                    Wh_out(2)
                if g == 2:
                    Wh_out(4)

            def sum_sq(g):
                bl = slice(16 * g, 16 * g + 16)
                need("i_sq", g + 1)
                dve.tensor_reduce(var0[:, bl], sq[:, bl, :], AX.X, ALU.add).then_inc(sem("i_sumsq"), 1)

            Wh_out(6)
            Wh_out(8)
            sum_sq(0)
            sum_sq(1)
            need("i_ps_UT")
            dve.tensor_copy(UTx[0:D, 0:D], psL[0:D, 0, 0:D]).then_inc(sem("i_UT"), 1)
            dve.tensor_copy(UTx[D:P, D:P], psL[D:P, 0, 0:D]).then_inc(sem("i_UT"), 1)
            Wh_out(10)
            sum_sq(2)
            Wh_out(12)
            sum_sq(3)
            need("i_sumsq", 4)
            dve.tensor_scalar(var0, var0, 1 / D, EPS, ALU.mult, ALU.add).then_inc(sem("i_var"), 1)
            need("i_var")
            rsqrt(rstd0, var0, total0, "i_rstd")
            need("i_rstd", 10)
            dve.tensor_scalar(rs1, rstd0, VMAX * LOW, None, ALU.mult).then_inc(sem("i_rs"), 1)
            dve.tensor_scalar(rs2, rstd0, VMAX, None, ALU.mult).then_inc(sem("i_rs"), 1)
            Wh_out(14)
            need("i_Wh_even", 8)
            need("i_Wh_odd", 8)
            dve.tensor_tensor(t0, Wh[:, :, D + 1], rstd0, ALU.mult).then_inc(sem("i_t"), 1)
            need("i_t")
            dve.tensor_reduce(tm, t0, AX.X, ALU.max).then_inc(sem("i_tm"), 1)
            dve.tensor_tensor(s0, Wh[:, :, D], rstd0, ALU.mult).then_inc(sem("i_s"), 1)
            need("i_ps_tT")
            dve.tensor_copy(tT, psL[0:D, 0, 0:P]).then_inc(sem("i_tT"), 1)
            need("i_ps_tm")
            dve.tensor_reduce(stT, psL[0:1, 1, 0:P], AX.X, ALU.max).then_inc(sem("i_stT"), 1)
            need("i_s")
            dve.tensor_scalar(ns[:], s0, -1.0, None, ALU.mult).then_inc(sem("i_neg_s"), 1)
            need("i_ps_T")
            dve.tensor_scalar(neg_T, psL[:, 1, 0:1], -1.0, None, ALU.mult).then_inc(sem("i_neg_T"), 1)
            dve.tensor_scalar(neg_T2, psL[:, 1, 0:1], -SLOPE, None, ALU.mult).then_inc(sem("i_neg_T"), 1)
            dve.tensor_copy(t_max, psL[:, 1, 0:1]).then_inc(sem("i_tmax"), 1)
            need("i_tmax")
            dve.tensor_scalar(z, s0, t_max, 1.0 - SLOPE, ALU.add, ALU.mult).then_inc(sem("i_z"), 1)
            need("i_z")
            dve.tensor_scalar(alpha[:], z, 0.0, None, ALU.min).then_inc(sem("i_z_alpha"), 1)
            dve.tensor_scalar(beta[:], z, -1.0, 0.0, ALU.mult, ALU.min).then_inc(sem("i_z_beta"), 1)

            def coded(lap, r):
                lap, r, u, n, _ = place(lap, r)
                slot, c = r // UB, r % UB
                if c == 0:
                    dve.wait_ge(landed[slot], 16 * (lap + 1))
                if isinstance(u, int) and u < UB:
                    need(f"tb_landed{u}", 16)
                after(dve, t_ready, u - QR + 1)
                dve.scalar_tensor_tensor(
                    out=Q[:, r % QR, :], in0=tb[:, UNIT * c:UNIT * c + UNIT], scalar=ns[:, bass.ds(n, 1)],
                    in1=ring[:, slot * N + UNIT * c:slot * N + UNIT * (c + 1)].bitcast(U8),
                    op0=ALU.is_gt, op1=ALU.add).then_inc(q_ready, 1)

            def mask2(lap, r):
                lap, r, u, _, _ = place(lap, r)
                dve.wait_ge(m1_ready, u + 1)
                dve.tensor_scalar(M[:, r % 2, 1, :], pT[r % 2], ONE8, None,
                                  ALU.is_equal).then_inc(m2_ready, 1)

            def post(lap, r):
                s, k = place(lap, r)[4] - 1, r % US
                recip, total, var, mean, rstd = (small[:, i, :] for i in (5, 6, 7, 3, 4))
                if k == 1:
                    need("p_den_g", s + 1)
                    dve.reciprocal(recip, small[:, 2, :]).then_inc(sem("d_recip"), 1)
                if k == 4:
                    need("p_x1", s + 1)
                    dve.tensor_reduce(total, xb[:], AX.X, ALU.add).then_inc(sem("d_sum"), 1)
                    need("d_sum", s + 1)
                    dve.tensor_scalar(mean, total, 1 / D, None, ALU.mult).then_inc(sem("d_mean"), 1)
                if k == 5:
                    need("p_sq", s + 1)
                    dve.tensor_reduce(total, p2[:], AX.X, ALU.add).then_inc(sem("d_sumsq"), 1)
                if k == 6:
                    need("d_sumsq", s + 1)
                    dve.tensor_scalar(var, total, 1 / D, EPS, ALU.mult, ALU.add).then_inc(sem("d_var"), 1)
                    need("d_var", s + 1)
                    guess(rstd, var, "d_half", "d_guess", s)

            need("i_e", 2)
            need("i_g", 5)
            need("i_rs", 2)
            dve.scalar_tensor_tensor(out=ev2, in0=e2, scalar=g_inv, in1=rs2, op0=ALU.mult,
                                     op1=ALU.mult).then_inc(sem("i_ev"), 1)
            dve.scalar_tensor_tensor(out=ev1, in0=e1, scalar=g_inv, in1=rs1, op0=ALU.mult,
                                     op1=ALU.mult).then_inc(sem("i_ev"), 1)
            need("i_ev", 2)
            need("i_neg_s")

            def v_part(c):
                tiles, buf = slice(UT * c, UT * c + UT), vt[c % 2]
                if c >= 2:
                    need("v_lo1", c - 1)
                    need("v_lo2", c - 1)
                dve.tensor_scalar(buf[:, 1, :, D], e2[:, tiles], VMAX, None, ALU.mult).then_inc(sem("v_te2"), 1)
                dve.tensor_scalar(buf[:, 0, :, D], e1[:, tiles], VMAX * LOW, None, ALU.mult).then_inc(sem("v_t1"), 1)
                dve.tensor_tensor(buf[:, 0, :, 0:D], Wh[:, tiles, 0:D], columns(ev1, tiles.start, tiles.stop, D),
                                  ALU.mult).then_inc(sem("v_t1"), 1)

            def v_low(c):
                tiles = slice(UT * c, UT * c + UT)
                need("v_hi1", c + 1)
                need("v_t1", 2 * c + 2)
                dve.scalar_tensor_tensor(out=V[:, tiles, DX:VW], in0=V[:, tiles, 0:DX], scalar=-LOW,
                                         in1=vt[c % 2][:, 0], op0=ALU.mult, op1=ALU.add).then_inc(sem("v_lo1"), 1)

            def unit(lap, r, ahead=True, post_too=True):
                if ahead:
                    coded(lap, r + 2)
                mask2(lap, r)
                if post_too:
                    post(lap, r)

            v_part(0)
            v_part(1)
            v_low(0)
            coded(0, 0)
            v_low(1)
            v_part(2)
            coded(0, 1)
            v_low(2)
            v_part(3)
            for r in range(BODY):
                unit(0, r, post_too=r >= US)
                if r == 0:
                    v_low(3)
                if r == 11:
                    need("i_ps_col", NB // 8)
                    dve.tensor_scalar(mean_col, ones[0:D, :], psL[0:D, 0, 0:1], 1 / N, ALU.mult,
                                      ALU.mult).then_inc(sem("i_mean_col"), 1)
                if r == 14:
                    need("i_ps_mean")
                    dve.tensor_scalar(meanW[:], psL[:, 0, 0:D], g_inv, 1.0, ALU.mult,
                                      ALU.mult).then_inc(sem("i_mean_Wh"), 1)
            with dve.Fori(1, NU // BODY) as lap:
                for r in range(BODY):
                    unit(lap, r)
            for r in range(NU % BODY):
                unit(NU // BODY, r, ahead=r + 2 < NU % BODY)

            steps = []

            def step(op):
                op.then_inc(sem("l_step"), 1)
                steps.append(op)
                need("l_step", len(steps))

            def over_d(v):
                return v.unsqueeze(2).broadcast_to([P, B, D])

            flag, den, den_g, mean, rstd, recip, total, var = (small[:, i, :] for i in range(8))
            v = att[:, :, 1, DX:VW]
            hi, lo = h2[:, (NS - 1) % 3, :, 0:D], h2[:, (NS - 1) % 3, :, DX:HW]
            need("h2_ready", NS - 1)
            need("att_ready", 2 * NB)
            step(dve.tensor_tensor(att[:, :, 0, :], att[:, :, 0, :], att[:, :, 1, :], ALU.add))
            step(dve.scalar_tensor_tensor(out=v, in0=att[:, :, 0, DX:VW], scalar=1 / LOW, in1=att[:, :, 0, 0:DX],
                                          op0=ALU.mult, op1=ALU.add))
            step(dve.tensor_scalar(flag, v[:, :, D], 0.0, None, ALU.is_equal))
            step(dve.tensor_tensor(den, v[:, :, D], flag, ALU.add))
            step(dve.tensor_scalar(den_g, den, g_inv, None, ALU.mult))
            step(dve.reciprocal(recip, den_g))
            step(dve.tensor_tensor(p1[:], meanW[:].unsqueeze(1).broadcast_to([P, B, D]), over_d(flag), ALU.mult))
            step(dve.tensor_tensor(p1[:], p1[:], v[:, :, 0:D], ALU.add))
            step(dve.tensor_tensor(p1[:], p1[:], over_d(recip), ALU.mult))
            dve.tensor_scalar(p2[:], p1[:], 0.0, None, ALU.min).then_inc(sem("l_mn"), 1)
            need("l_mn")
            step(dve.tensor_tensor(p1[:], p1[:], p2[:], ALU.subtract))
            need("xb_landed", 16 * NS)
            step(dve.tensor_tensor(p1[:], xb[:], p1[:], ALU.add))
            need("l_exp")
            dve.scalar_tensor_tensor(out=xb[:], in0=p3, scalar=-1.0, in1=p1[:], op0=ALU.add,
                                     op1=ALU.add).then_inc(sem("l_x1"), 1)
            need("l_x1")
            step(dve.tensor_reduce(total, xb[:], AX.X, ALU.add))
            step(dve.tensor_scalar(mean, total, 1 / D, None, ALU.mult))
            step(dve.tensor_tensor(p1[:], xb[:], over_d(mean), ALU.subtract))
            step(dve.tensor_tensor(p2[:], p1[:], p1[:], ALU.mult))
            step(dve.tensor_reduce(total, p2[:], AX.X, ALU.add))
            step(dve.tensor_scalar(var, total, 1 / D, EPS, ALU.mult, ALU.add))
            rsqrt(rstd, var, total, "l_rstd")
            need("l_rstd", 10)
            step(dve.scalar_tensor_tensor(out=p2[:], in0=p1[:], scalar=0.0, in1=over_d(rstd), op0=ALU.max, op1=ALU.mult))
            step(dve.tensor_scalar(hi, p2[:], HSCALE, None, ALU.mult))
            dve.scalar_tensor_tensor(out=lo, in0=p2[:], scalar=HSCALE, in1=hi, op0=ALU.mult,
                                     op1=ALU.subtract).then_inc(sem("h2_ready"), 1)

            def add(u):
                v = u - (NU - US)
                for part in range(2):
                    for i in range(2):
                        g = 2 * u + i
                        ct = GT * (g % (NB // GT))
                        bank = psL[:, i] if (u - ND) % 2 else psT[:, 2 + i]
                        ps = bank[:, 0:GW].rearrange("p (t w) -> p t w", w=HW)
                        if part == 0:
                            need("l2_done", g + 1)
                            before = g - NB // GT
                            if before < 2 * ND:
                                need("added", 1 + 2 * (before + 1))
                            else:
                                need("f_added", before - 2 * ND + 1)
                            dve.tensor_tensor(acc[:, ct:ct + GT, :], acc[:, ct:ct + GT, :], ps[:, :, 0:DX],
                                              ALU.add).then_inc(sem("f_high"), 1)
                        else:
                            need("f_high", g - 2 * ND + 1)
                            to = acc[:, ct:ct + GT, 0:D] if v < 0 else fin[:, v // 2 % 2, ct % 8:ct % 8 + GT, :]
                            dve.tensor_tensor(to, acc[:, ct:ct + GT, 0:D], ps[:, :, DX:HW],
                                              ALU.add).then_inc(sem("f_added"), 1)

            for u in range(ND, NU - US):
                add(u)
            for f in range(9):
                if f < 8:
                    after(dve, sem("f_T"), f - 1)
                    add(NU - US + 2 * f)
                    add(NU - US + 2 * f + 1)
                    tiles = slice(8 * f, 8 * f + 8)
                    dve.reciprocal(rdeg[:, tiles], acc[:, tiles, D]).then_inc(sem("f_rdeg"), 1)
                if f:
                    tiles = slice(8 * f - 8, 8 * f)
                    need("f_z", f)
                    need("f_rdeg", f)
                    dve.tensor_tensor(outs[:, tiles, :], psA[:, (f - 1) % 2, :].rearrange("p (t d) -> p t d", t=8),
                                      columns(rdeg, tiles.start, tiles.stop, D), ALU.mult).then_inc(sem("f_mean"), 1)
                    need("f_mean", f)
                    need("f_x1", f)
                    dve.scalar_tensor_tensor(out=outs[:, tiles, :], in0=outs[:, tiles, :], scalar=0.0,
                                             in1=x1s[:, tiles, :], op0=ALU.max, op1=ALU.add).then_inc(sem("f_out"), 1)

        @block.scalar
        def _(act):
            def need(name, count=1):
                act.wait_ge(sem(name), count)

            def wh_out(g):
                need("i_ps_Wh", g + 1)
                act.activation(Wh[:, 4 * g:4 * g + 4, :].rearrange("p b n -> p (b n)"),
                               psA[:, 1, 0:4 * (D + 2)], ACT.Copy).then_inc(sem("i_Wh_odd"), 1)

            xg = x.rearrange("(g b p) d -> g p b d", p=P, g=4)
            with nc.allow_non_contiguous_dma(reason="128 numbers"):
                act.dma_start(a12, a.rearrange("(t f) o -> f (t o)", t=2)).then_inc(sem("w_landed"), 16)
            for g in (1, 3):
                act.dma_start(xs[:, 16 * g:16 * g + 16, :], xg[g]).then_inc(sem(f"x_landed{g}"), 16)
            for g in range(8):
                need("i_ps_hT", g + 1)
                act.activation(hT[:, 4 * g:4 * g + 4, :].rearrange("p b n -> p (b n)"), psT[:, g % 4, :],
                               ACT.Relu).then_inc(sem("i_hT"), 1)
                if g:
                    wh_out(2 * g - 1)
                if 3 <= g < 7:
                    q, bl = g - 3, slice(16 * (g - 3), 16 * (g - 3) + 16)
                    need(("i_xc_dve", "i_xc_pool")[q % 2], q // 2 + 1)
                    act.activation(sq[:, bl, :], xs[:, bl, :], ACT.Square).then_inc(sem("i_sq"), 1)
            wh_out(15)
            need("i_neg_T", 2)
            act.activation(e2, t0, ACT.Exp, bias=neg_T2, scale=SLOPE).then_inc(sem("i_e"), 1)
            act.activation(e1, t0, ACT.Exp, bias=neg_T).then_inc(sem("i_e"), 1)

            def v_high(c):
                tiles, buf = slice(UT * c, UT * c + UT), vt[c % 2]
                need("v_t2", c + 1)
                need("v_te2", c + 1)
                act.activation(V[:, tiles, VW:VW + DX], buf[:, 1], ACT.Copy).then_inc(sem("v_hi2"), 1)
                need("v_t1", 2 * c + 2)
                act.activation(V[:, tiles, 0:DX], buf[:, 0], ACT.Copy, scale=1 / LOW).then_inc(sem("v_hi1"), 1)

            def v_low(c):
                tiles, buf = slice(UT * c, UT * c + UT), vt[c % 2]
                need("v_rest2", c + 1)
                act.activation(V[:, tiles, VW + DX:2 * VW], buf[:, 1], ACT.Copy, scale=LOW).then_inc(sem("v_lo2"), 1)

            v_high(0)
            v_high(1)
            v_low(0)
            v_low(1)
            v_high(2)
            need("i_z_alpha")
            act.activation(alpha[:], alpha[:], ACT.Exp).then_inc(sem("i_alpha"), 1)
            need("i_z_beta")
            act.activation(beta[:], beta[:], ACT.Exp).then_inc(sem("i_beta"), 1)
            need("i_m56")
            need("i_alpha")
            need("i_beta")

            def mask1(lap, r):
                _, r, u, _, _ = place(lap, r)
                after(act, l1_done, u - 1)
                act.wait_ge(t_ready, u + 1)
                act.activation(M[:, r % 2, 0, :], pT[r % 2], ACT.Relu, bias=m56).then_inc(m1_ready, 1)

            def scaled(lap, r):
                _, r, u, n, s = place(lap, r - UB)
                act.wait_ge(l1_done, u + UB)
                if (r // UB) % B == 0:
                    after(act, sem("p_x1"), s)
                for k, factor in enumerate((alpha, beta)):
                    act.activation(att[:, (r // UB) % B, k, :], psA[:, (r // UB) % 2, VW * k:VW * k + VW],
                                   ACT.Copy, scale=factor[:, bass.ds(n, 1)]).then_inc(att_ready, 1)

            def staged(lap, r):
                _, r, u, _, _ = place(lap, r - 1 - LAG)
                for i in range(2):
                    act.wait_ge(l2_done, 2 * u + i + 1)
                    after(act, added, 1 + 2 * (2 * u + i - STAGE + 1))
                    act.activation(stage[:, (2 * r + i) % STAGE].rearrange("p t w -> p (t w)"),
                                   psL[:, i, 0:GW], ACT.Copy).then_inc(stage_ready, 1)

            def post(lap, r):
                s, k = place(lap, r)[4] - 1, r % US
                if k == 2:
                    need("p_hp", s + 1)
                    act.activation(p2[:], p1[:], ACT.Relu, scale=-1.0).then_inc(sem("a_neg"), 1)
                    need("a_neg", s + 1)
                    act.activation(p3, p2[:], ACT.Exp, scale=-1.0).then_inc(sem("a_exp"), 1)
                if k == 5:
                    need("p_sq", s + 1)
                    act.activation(p1[:], p1[:], ACT.Relu, scale=HSCALE).then_inc(sem("a_relu"), 1)

            def unit(lap, r, first=False):
                mask1(lap, r)
                if r % UB == 0 and not (first and r == 0):
                    scaled(lap, r)
                if not first or r > LAG:
                    staged(lap, r)
                if not first or r >= US:
                    post(lap, r)

            for r in range(BODY):
                unit(0, r, first=True)
                if r == 0:
                    v_low(2)
                    v_high(3)
                if r == 1:
                    v_low(3)
            with act.Fori(1, NU // BODY) as lap:
                for r in range(BODY):
                    unit(lap, r)
            for r in range(NU % BODY):
                unit(NU // BODY, r)
            scaled(NU // BODY, NU % BODY)
            for u in range(NU - 1 - LAG, ND):
                staged(NU // BODY, NU % BODY + u - (NU - 1 - LAG))
                if u == NU - LAG:
                    need("l_mn")
                    act.activation(p3, p2[:], ACT.Exp).then_inc(sem("l_exp"), 1)

            for f in range(8):
                need("f_T", f + 1)
                after(act, sem("f_z"), f - 1)
                act.activation(aggT[:, f % 2, :], psT[:, f % 2, :], ACT.Copy).then_inc(sem("f_aggT"), 1)

        @block.tensor
        def _(pe):
            def need(name, count=1):
                pe.wait_ge(sem(name), count)

            need("i_ident", 2)
            need("w_landed", 48)
            pe.transpose(psA[0:D, 0, 0:D], Wx[0:D, 0:D], identf[0:D, 0:D]).then_inc(sem("i_ps_WT"), 1)
            need("i_WT", 2)
            pe.matmul(psA[:, 1, 0:2], WT2, a12, start=True, stop=True).then_inc(sem("i_ps_Wa"), 1)
            need("i_Wsq")
            need("i_ones")
            pe.matmul(psL[:, 1, 0:D], ones[0:D, :], Wsq, start=True, stop=True).then_inc(sem("i_ps_norm"), 1)

            def h_transposed(g):
                if g % 2 == 0:
                    need(("i_xc_dve", "i_xc_pool")[g // 2 % 2], g // 4 + 1)
                after(pe, sem("i_hT"), g - 3)
                for i in range(4):
                    last = pe.transpose(psT[:, g % 4, P * i:P * i + P],
                                        xs[:, 8 * g + 2 * i:8 * g + 2 * i + 2, :].rearrange("p b d -> p (b d)"),
                                        identf[:])
                last.then_inc(sem("i_ps_hT"), 1)

            h_transposed(0)
            for g in range(16):
                if g % 2 == 0:
                    if g < 14:
                        h_transposed(g // 2 + 1)
                    need("i_hT", g // 2 + 1)
                if g == 0:
                    need("i_Wa", 2)
                if g >= 2:
                    need("i_Wh_odd" if g % 2 else "i_Wh_even", (g - 2) // 2 + 1)
                for i in range(2):
                    last = pe.matmul(psA[:, g % 2, i * 2 * (D + 2):(i + 1) * 2 * (D + 2)], hT[:, 2 * g + i, :], Wx,
                                     start=True, stop=True, skip_group_check=True)
                last.then_inc(sem("i_ps_Wh"), 1)
                if g == 9:
                    need("u_landed", 32)
                    pe.transpose(psL[:, 0, 0:D], UU, identf[0:D, 0:D]).then_inc(sem("i_ps_UT"), 1)
            need("i_t")
            need("i_UT", 2)
            pe.transpose(psL[0:D, 0, 0:P], t0, identf[:]).then_inc(sem("i_ps_tT"), 1)
            need("i_tm")
            need("i_g", 1)
            pe.transpose(psL[0:1, 1, 0:P], tm, identf[:]).then_inc(sem("i_ps_tm"), 1)
            need("i_stT")
            pe.matmul(psL[:, 1, 0:1], ones[0:1, :], stT, start=True, stop=True).then_inc(sem("i_ps_T"), 1)
            def column_sum(b):
                if b == 0:
                    need("i_tT")
                for i in range(b, b + 8):
                    last = pe.matmul(psL[0:D, 0, 0:1], Wh[:, i, 0:D], rstd0[:, i:i + 1], start=(i == 0),
                                     stop=(i == NB - 1), skip_group_check=True)
                last.then_inc(sem("i_ps_col"), 1)

            def transposes(lap, r):
                _, r, u, _, _ = place(lap, r)
                pe.wait_ge(q_ready, u + 1)
                after(pe, m2_ready, u - 1)
                for i in range(UT):
                    last = pe.transpose(pT[r % 2][:, P * i:P * i + P], Q[:, r % QR, P * i:P * i + P], ident[:])
                last.then_inc(t_ready, 1)

            def attend(lap, r, first):
                _, r, u, n, _ = place(lap, r)
                c = r % UB
                if c == 0:
                    after(pe, att_ready, 2 * (n - 1))
                if first and r < UB:
                    need("v_lo1", r + 1)
                    need("v_lo2", r + 1)
                pe.wait_ge(m2_ready, u + 1)
                for i in range(UT):
                    for k in range(2):
                        last = pe.matmul(psA[:, (r // UB) % 2, VW * k:VW * k + VW],
                                         M[:, r % 2, k, P * i:P * i + P],
                                         V[:, UT * c + i, VW * k:VW * k + VW],
                                         start=(c == 0 and i == 0 and k == 0), stop=(c == UB - 1 and i == UT - 1),
                                         skip_group_check=True)
                last.then_inc(l1_done, 1)

            def sums_wait(lap, r):
                _, r, u, _, s = place(lap, r)
                if r % US == 0:
                    need("h2_ready", s + 1)
                    need("i_mean_Wh")
                if not isinstance(u, int):
                    pe.wait_ge(stage_ready, 2 * u)
                elif u < ND or u == ND + 1:
                    after(pe, stage_ready, min(2 * u, 2 * ND))
                elif u == ND:
                    pe.wait_ge(m2_ready, NU)
                else:
                    pe.wait_ge(sem("f_added"), 2 * (u - 1 - ND))

            def sum_bank(u, i):
                return psT[:, 2 + i] if isinstance(u, int) and u >= ND and (u - ND) % 2 == 0 else psL[:, i]

            def sums(lap, r):
                _, r, u, _, _ = place(lap, r)
                s0 = (r // US) * B
                for i in range(2):
                    for t in range(GT):
                        ct = 2 * GT * (r % US) + GT * i + t
                        for b in range(B):
                            slot = s0 + b
                            last = pe.matmul(sum_bank(u, i)[:, HW * t:HW * t + HW],
                                             ring[:, slot * N + ct * P:slot * N + ct * P + P],
                                             h2[:, (r // US) % 3, b, :],
                                             start=(t == 0 and b == 0), stop=(b == B - 1), skip_group_check=True)
                    last.then_inc(l2_done, 1)

            def unit(lap, r, first=False, ahead=True):
                if ahead:
                    transposes(lap, r + 1)
                two = not first or r >= LAG
                if two:
                    sums_wait(lap, r - LAG)
                attend(lap, r, first)
                if two:
                    sums(lap, r - LAG)

            transposes(0, 0)
            for r in range(BODY):
                unit(0, r, first=True)
                if 2 <= r < 2 + NB // 8:
                    column_sum(8 * (r - 2))
                if r == 12:
                    need("i_mean_col")
                    pe.matmul(psL[:, 0, 0:D], mean_col, identf[0:D, 0:D], start=True,
                              stop=True).then_inc(sem("i_ps_mean"), 1)
            with pe.Fori(1, NU // BODY) as lap:
                for r in range(BODY):
                    unit(lap, r)
            for r in range(NU % BODY):
                unit(NU // BODY, r, ahead=r + 1 < NU % BODY)
            for r in range(NU % BODY, NU % BODY + LAG - US):
                sums_wait(NU // BODY, r - LAG)
                sums(NU // BODY, r - LAG)

            for f in range(9):
                if f < 8:
                    r = NU % BODY - US + 2 * f
                    sums_wait(NU // BODY, r)
                    sums(NU // BODY, r)
                if f:
                    e = f - 1
                    need("f_added", 2 * (DIRECT - US) + 4 * f)
                    after(pe, sem("f_aggT"), e - 1)
                    for i in range(4):
                        last = pe.transpose(psT[:, e % 2, P * i:P * i + P],
                                            fin[:, e % 2, 2 * i:2 * i + 2, :].rearrange("p t d -> p (t d)"), identf[:])
                    last.then_inc(sem("f_T"), 1)
                if f < 8:
                    sums_wait(NU // BODY, r + 1)
                    sums(NU // BODY, r + 1)
                if f:
                    need("f_aggT", f)
                    after(pe, sem("f_mean"), e - 1)
                    if e == 0:
                        need("att_ready", 2 * NB)
                    for i in range(4):
                        last = pe.matmul(psA[:, e % 2, P * i:P * i + P], aggT[:, e % 2, P * i:P * i + P], UTx[:],
                                         start=True, stop=True, skip_group_check=True)
                    last.then_inc(sem("f_z"), 1)


INPUTS = ["x", "adj", "L0_gnn_W", "L0_gnn_a", "L1_gnn_U"]


def kernel(**inputs):
    import numpy as np
    import concourse.bacc as bacc
    from concourse.bass_utils import run_bass_kernel_spmd

    nc = bacc.Bacc("TRN2", target_bir_lowering=False, num_devices=1, dynamic_dma_scratch_size=2048)
    arrays, args = {}, []
    for name in INPUTS:
        arrays[name] = np.ascontiguousarray(inputs[name])
        args.append(nc.dram_tensor(name, arrays[name].shape, mybir.dt.from_np(arrays[name].dtype),
                                   kind="ExternalInput").ap())
    x1_dram = nc.dram_tensor("x1_dram", (N, D), F32, kind="Internal").ap()
    t_dram = nc.dram_tensor("t_dram", (NB, P), F32, kind="Internal").ap()
    out = nc.dram_tensor("out", (N, D), F32, kind="ExternalOutput").ap()
    build(nc, *args, x1_dram, t_dram, out)
    return run_bass_kernel_spmd(nc, [arrays], core_ids=[0]).results[0]["out"]
```
